# Optimizing a Trainium2 kernel written in Bass

```python
import numpy as np
import jax
import jax.numpy as jnp

def _softmax(x, axis=-1):
    return jax.nn.softmax(x, axis=axis)

def _gelu(x):
    return jax.nn.gelu(x, approximate=True)

def _silu(x):
    return jax.nn.silu(x)

def _sigmoid(x):
    return jax.nn.sigmoid(x)

def _layernorm(x, axis=-1, eps=1e-05):
    m = jnp.mean(x, axis=axis, keepdims=True)
    v = jnp.var(x, axis=axis, keepdims=True)
    return (x - m) / jnp.sqrt(v + eps)

def _scatter_add(tgt, idx, src, axis=0):
    return tgt.at[idx].add(src)

def _segment_sum(src, seg, n):
    return jax.ops.segment_sum(src, seg, n)
kernel_name = 'mk_gnn_resnorm_d2_gnn_r8_460da1'

def setup_inputs(seed: int=0):
    np.random.seed(seed)
    _w = jnp.asarray

    def _rec_inputs():
        import jax
        import jax.numpy as jnp
        _gk = jax.random.key(seed)
        x = -0.000202 + 1 * jax.random.normal(jax.random.fold_in(_gk, 1), (12500, 64), jnp.float32)
        src = jax.random.randint(jax.random.fold_in(_gk, 2), (400000,), 0, 12500, jnp.int32)
        dst = jnp.minimum((12500 * jax.random.uniform(jax.random.fold_in(_gk, 3), (400000,)) ** 2.0).astype(jnp.int32), 99999)
        _o = jnp.argsort(dst, stable=True)
        src = src[_o]
        dst = dst[_o]
        edge_attr_3 = jax.random.uniform(jax.random.fold_in(_gk, 12), (400000, 3), jnp.float32, 0.0, 1)
        return (x, src, dst, edge_attr_3)
    x, src, dst, edge_attr_3 = _rec_inputs()

    def _L0_gnn_setup():
        import jax, jax.numpy as jnp
        import numpy as np
        N_NODES = 12500
        N_EDGES = 125000
        IN_DIM = 64
        OUT_DIM = 64
        ATTR_DIM = 3
        K = 3
        EPS = 1e-14

        def _gmm_conv(x, src, dst, edge_attr, g, mu, sigma, root_w, bias):
            E = edge_attr.shape[0]
            diff = edge_attr[:, None, :] - mu[None, :, :]
            gauss = jnp.exp(jnp.sum(-0.5 * diff * diff / (EPS + sigma[None] ** 2), axis=-1))
            xj = x[src] @ g
            msg = jnp.einsum('eko,ek->eo', xj.reshape(E, K, OUT_DIM), gauss)
            summed = jax.ops.segment_sum(msg, dst, num_segments=N_NODES)
            cnt = jax.ops.segment_sum(jnp.ones((E,), x.dtype), dst, num_segments=N_NODES)
            aggr = summed / jnp.maximum(cnt, 1.0)[:, None]
            return aggr + x @ root_w + bias
        key = jax.random.key(seed)
        ks = jax.random.split(key, 8)
        x = jax.random.normal(ks[0], (N_NODES, IN_DIM), dtype=jnp.float32)
        edge_index = jax.random.randint(ks[1], (2, N_EDGES), 0, N_NODES, dtype=jnp.int64)
        edge_attr = jax.random.uniform(ks[2], (N_EDGES, ATTR_DIM), dtype=jnp.float32)
        g = jax.random.normal(ks[3], (IN_DIM, K * OUT_DIM), dtype=jnp.float32) / np.sqrt(IN_DIM)
        mu = jax.random.normal(ks[4], (K, ATTR_DIM), dtype=jnp.float32) * 0.5
        sigma = jnp.ones((K, ATTR_DIM), dtype=jnp.float32)
        root_w = jax.random.normal(ks[5], (IN_DIM, OUT_DIM), dtype=jnp.float32) / np.sqrt(IN_DIM)
        bias = jnp.zeros((OUT_DIM,), dtype=jnp.float32)
        return {'x': x, 'edge_index': edge_index, 'edge_attr': edge_attr, 'g': g, 'mu': mu, 'sigma': sigma, 'root_w': root_w, 'bias': bias}
    _L0_gnn_all = _L0_gnn_setup()
    _L0_gnn_in = {k: v for k, v in _L0_gnn_all.items() if k in ('g', 'mu', 'sigma', 'root_w', 'bias')}
    del _L0_gnn_all

    def _L1_gnn_setup():
        import jax, jax.numpy as jnp
        import numpy as np
        N_NODES = 12500
        N_EDGES = 200000
        IN_F, HID_F, OUT_F = (64, 64, 64)

        def _sage_conv(h, W_self, W_neigh, b, edge_src, edge_dst, n_nodes):
            msg = h[edge_src]
            nbr_sum = jax.ops.segment_sum(msg, edge_dst, num_segments=n_nodes)
            deg = jax.ops.segment_sum(jnp.ones((edge_dst.shape[0],), h.dtype), edge_dst, num_segments=n_nodes)
            nbr_mean = nbr_sum / jnp.maximum(deg, 1.0)[:, None]
            return h @ W_self + nbr_mean @ W_neigh + b
        key = jax.random.key(seed)
        ks = jax.random.split(key, 9)
        s = 1.0 / np.sqrt(IN_F)
        return {'feats': jax.random.normal(ks[0], (N_NODES, IN_F), jnp.float32), 'W_self1': jax.random.normal(ks[1], (IN_F, HID_F), jnp.float32) * s, 'W_neigh1': jax.random.normal(ks[2], (IN_F, HID_F), jnp.float32) * s, 'b1': jax.random.normal(ks[3], (HID_F,), jnp.float32) * s, 'W_self2': jax.random.normal(ks[4], (HID_F, OUT_F), jnp.float32) * s, 'W_neigh2': jax.random.normal(ks[5], (HID_F, OUT_F), jnp.float32) * s, 'b2': jax.random.normal(ks[6], (OUT_F,), jnp.float32) * s, 'edge_src': jax.random.randint(ks[7], (N_EDGES,), 0, N_NODES, jnp.int64), 'edge_dst': jax.random.randint(ks[8], (N_EDGES,), 0, N_NODES, jnp.int64)}
    _L1_gnn_all = _L1_gnn_setup()
    _L1_gnn_in = {k: v for k, v in _L1_gnn_all.items() if k in ('W_self1', 'W_neigh1', 'b1', 'W_self2', 'W_neigh2', 'b2')}
    del _L1_gnn_all
    return {'x': x, 'src': src, 'dst': dst, 'edge_attr_3': edge_attr_3, 'L0_gnn_g': _L0_gnn_in['g'], 'L0_gnn_mu': _L0_gnn_in['mu'], 'L0_gnn_sigma': _L0_gnn_in['sigma'], 'L0_gnn_root_w': _L0_gnn_in['root_w'], 'L0_gnn_bias': _L0_gnn_in['bias'], 'L1_gnn_W_self1': _L1_gnn_in['W_self1'], 'L1_gnn_W_neigh1': _L1_gnn_in['W_neigh1'], 'L1_gnn_b1': _L1_gnn_in['b1'], 'L1_gnn_W_self2': _L1_gnn_in['W_self2'], 'L1_gnn_W_neigh2': _L1_gnn_in['W_neigh2'], 'L1_gnn_b2': _L1_gnn_in['b2']}

def reference(x, src, dst, edge_attr_3, L0_gnn_g, L0_gnn_mu, L0_gnn_sigma, L0_gnn_root_w, L0_gnn_bias, L1_gnn_W_self1, L1_gnn_W_neigh1, L1_gnn_b1, L1_gnn_W_self2, L1_gnn_W_neigh2, L1_gnn_b2):
    import jax
    import jax.numpy as jnp

    def _L0_gnn_ref(x, edge_index, edge_attr, g, mu, sigma, root_w, bias):
        import jax, jax.numpy as jnp
        import numpy as np
        N_NODES = 12500
        N_EDGES = 125000
        IN_DIM = 64
        OUT_DIM = 64
        ATTR_DIM = 3
        K = 3
        EPS = 1e-14

        def _gmm_conv(x, src, dst, edge_attr, g, mu, sigma, root_w, bias):
            E = edge_attr.shape[0]
            diff = edge_attr[:, None, :] - mu[None, :, :]
            gauss = jnp.exp(jnp.sum(-0.5 * diff * diff / (EPS + sigma[None] ** 2), axis=-1))
            xj = x[src] @ g
            msg = jnp.einsum('eko,ek->eo', xj.reshape(E, K, OUT_DIM), gauss)
            summed = jax.ops.segment_sum(msg, dst, num_segments=N_NODES)
            cnt = jax.ops.segment_sum(jnp.ones((E,), x.dtype), dst, num_segments=N_NODES)
            aggr = summed / jnp.maximum(cnt, 1.0)[:, None]
            return aggr + x @ root_w + bias
        src, dst = (edge_index[0], edge_index[1])
        h = x
        out = _gmm_conv(x, src, dst, edge_attr, g, mu, sigma, root_w, bias)
        return jax.nn.silu(out + h)

    def _L1_gnn_ref(feats, W_self1, W_neigh1, b1, W_self2, W_neigh2, b2, edge_src, edge_dst):
        import jax, jax.numpy as jnp
        import numpy as np
        N_NODES = 12500
        N_EDGES = 200000
        IN_F, HID_F, OUT_F = (64, 64, 64)

        def _sage_conv(h, W_self, W_neigh, b, edge_src, edge_dst, n_nodes):
            msg = h[edge_src]
            nbr_sum = jax.ops.segment_sum(msg, edge_dst, num_segments=n_nodes)
            deg = jax.ops.segment_sum(jnp.ones((edge_dst.shape[0],), h.dtype), edge_dst, num_segments=n_nodes)
            nbr_mean = nbr_sum / jnp.maximum(deg, 1.0)[:, None]
            return h @ W_self + nbr_mean @ W_neigh + b
        n = feats.shape[0]
        h = _sage_conv(feats, W_self1, W_neigh1, b1, edge_src, edge_dst, n)
        h = jax.nn.relu(h)
        return _sage_conv(h, W_self2, W_neigh2, b2, edge_src, edge_dst, n)
    edge_index = jnp.stack([src, dst])
    x = _layernorm(x + _L0_gnn_ref(x, edge_index, edge_attr_3, L0_gnn_g, L0_gnn_mu, L0_gnn_sigma, L0_gnn_root_w, L0_gnn_bias), axis=-1)
    x = _layernorm(x + _L1_gnn_ref(x, L1_gnn_W_self1, L1_gnn_W_neigh1, L1_gnn_b1, L1_gnn_W_self2, L1_gnn_W_neigh2, L1_gnn_b2, src, dst), axis=-1)
    return x

_drawn_inputs = setup_inputs


def setup_inputs(seed=0):
    import zlib

    import numpy as np

    out = dict(_drawn_inputs(seed))
    spreads = {'L0_gnn_sigma': (1.0, 0.2), 'L0_gnn_bias': (0.0, 0.1)}
    factors = {}
    for name, (base, spread) in spreads.items():
        noise = np.random.default_rng([zlib.crc32(name.encode()), seed]).standard_normal(out[name].shape)
        drawn = base * np.exp(spread * noise) if base else spread * noise
        out[name] = jnp.asarray(drawn.astype(out[name].dtype))
    for name, factor in factors.items():
        out[name] = (out[name] * factor).astype(out[name].dtype)
    return out
```

```python
from contextlib import ExitStack

import concourse.bass as bass
from concourse import mybir

F32 = mybir.dt.float32
I32 = mybir.dt.int32
ALU = mybir.AluOpType
ACT = mybir.ActivationFunctionType
AX_X = mybir.AxisListType.X

P = 128
D = 64
K = 3
A = 3
TN = 125
LN_EPS = 1e-5
SIGMA_EPS = 1e-14


def gnn_kernel(nc, x, src, dst, attr, g, mu, sigma, root_w, bias, w_self1, w_neigh1, b1,
               w_self2, w_neigh2, b2, out):
    N = x.shape[0]
    E = src.shape[0]
    NT = N // TN
    NB = E // P
    CH = 125
    BC = NB // CH
    SB = 5
    NS = BC // SB
    GT = 4
    NG = NT // GT
    assert NT * TN == N and NB * P == E and CH * BC == NB and NS * SB == BC and NG * GT == NT
    AW = K * D + 1

    table1 = nc.dram_tensor("table_x1", [N, D], F32).ap()
    table2 = nc.dram_tensor("table_h", [N, D], F32).ap()

    with ExitStack() as ctx:
        def sb(name, shape, dt=F32):
            return ctx.enter_context(nc.sbuf_tensor(name, shape, dt))

        def ps(name, shape):
            return ctx.enter_context(nc.psum_tensor(name, shape, F32))

        def sem(name):
            return ctx.enter_context(nc.semaphore(name))

        src_col = sb("src_col", [P, NB], I32)
        dst_col = sb("dst_col", [P, NB])
        w_col = sb("w_col", [P, K, NB])
        acc = sb("acc", [P, NT, AW])
        gath = sb("gath", [P, 2, BC, D])
        wgath = sb("wgath", [P, BC, AW])
        onehot = sb("onehot", [P, NS, SB, P])
        idx = sb("idx", [P, 2, BC], I32)
        local = sb("local", [P, BC])

        acc_flat = acc[:].rearrange("p t a -> p (t a)")
        attr_nat = acc_flat[0:CH, 0:A * BC * P].rearrange("p (e a) -> p e a", a=A)
        w_nat = acc_flat[0:CH, A * BC * P:2 * A * BC * P].rearrange("p (k e) -> p k e", k=K)
        dst_nat = wgath[:].rearrange("p b a -> p (b a)")[0:CH, 0:BC * P]
        src_nat = gath[:].rearrange("p s b d -> p (s b d)")[0:CH, 0:BC * P]
        sq_nat = onehot[:].rearrange("p n b c -> p (n b c)")[0:CH, 0:BC * P]
        assert 2 * A * BC * P <= NT * AW and BC * P <= BC * AW

        musig = sb("musig", [P, 2, K * A])
        consts = sb("consts", [P, 4, K * A])
        iota = sb("iota", [P, P])
        pidx = sb("pidx", [P, 1])
        ident = sb("ident", [P, P])
        later = sb("later", [P, P])
        tile_base = sb("tile_base", [P, NT])
        span = sb("span", [P, 2])
        spi = sb("spi", [P, 2], I32)
        sq_t = sb("sq_t", [P, 2])
        fix = sb("fix", [P, 2])
        win = sb("win", [P, 2])
        win_tab = sb("win_tab", [1, 3, P], I32)
        cat = sb("cat", [P, 2, GT, 2 * P])
        catT = sb("catT", [P, 2, 2, GT, TN])
        bias_t = sb("bias_t", [P, 3, D])
        w0 = sb("w0", [P, 2, D])
        w1 = sb("w1", [P, D])
        w2 = sb("w2", [P, D])
        rcount = sb("rcount", [P, NT])
        stat = sb("stat", [P, 4, NT])
        eps_t = sb("eps_t", [P, 1])

        sums = ps("sums", [P, 512])
        ptr = [[ps(f"ptr{s}{h}", [P, 512]) for h in range(2)] for s in range(2)]
        pout = [ps(f"pout{s}", [P, 512]) for s in range(2)]

        s_load = sem("s_load")
        s_src = sem("s_src")
        s_attr = sem("s_attr")
        s_const = sem("s_const")
        s_pre = sem("s_pre")
        s_sq = sem("s_sq")
        s_wexp = sem("s_wexp")
        s_nat = [sem(f"s_nat{f}") for f in range(5)]
        s_tr = sem("s_tr")
        s_evv = sem("s_evv")
        s_eva = sem("s_eva")
        s_wt = sem("s_wt")
        s_wp = sem("s_wp")
        s_tab = sem("s_tab")
        s_v = sem("s_v")
        s_table = sem("s_table")
        passes = []
        for p in range(3):
            passes.append({k: sem(f"s{p}_{k}") for k in (
                "idx", "gath0", "gath1", "gfree", "wg", "local", "oh", "ohused", "added", "done")})
        epis = []
        for p in range(3):
            epis.append({k: sem(f"e{p}_{k}") for k in (
                "x0", "x1", "cata", "catv", "tr", "eva", "evv", "mm", "z", "keep", "fin", "finv", "fina", "seq")})
        s_out = sem("s_out")
        s_tick = sem("s_tick")

        block = ctx.enter_context(nc.Block())

        FIELDS = 5
        EV = [(k, min(4, BC - k)) for k in range(0, BC, 4)]
        evs = [(f, k, m) for f in range(FIELDS) for k, m in EV]
        nats = [src_nat, dst_nat] + [w_nat[:, k, :] for k in range(K)]
        cols = [src_col[:], dst_col[:]] + [w_col[:, k, :] for k in range(K)]
        banks = [ptr[0][0], ptr[0][1], ptr[1][0], ptr[1][1]]

        def pairs(eng, n, body):
            with eng.Fori(0, n // 2, 1) as i:
                body(i * 2, 0, i)
                body(i * 2 + 1, 1, i)
            if n % 2:
                body(n - 1, 0, n // 2)

        tables = [x, table1, table2]

        def evacuate(eng, n, f, k, m, done):
            eng.wait_ge(s_tr, n + 1)
            o = cols[f].rearrange("p (q k) -> p k q", k=BC)[:, k:k + m, :]
            i = banks[n % 4][:, 0:m * CH].rearrange("p (k q) -> p k q", k=m)
            (eng.copy if eng is nc.scalar else eng.tensor_copy)(o, i).then_inc(done, 1)

        def epilogue_act(act, n):
            e = epis[n]
            last = 2 * D if n == 0 else 0

            def group(c, s, i):
                if n:
                    own = 0 if n == 1 else 2 * D
                    act.wait_ge(passes[n]["done"], 1)
                    act.wait_ge(e["tr"], c + 1)
                    act.copy(cat[0:TN, s, :, 0:D],
                             acc[0:TN, bass.ds(c * GT, GT), own:own + D]).then_inc(e["cata"], 1)
                act.wait_ge(e["tr"], c + 3)
                act.copy(catT[:, s, 0], ptr[s][0][:, 0:GT * TN].rearrange("p (t q) -> p t q", t=GT)).then_inc(e["eva"], 1)
                if n == 0:
                    act.wait_ge(e["catv"], c + 1)
                    act.copy(acc[0:TN, bass.ds(c * GT, GT), D:2 * D],
                             cat[0:TN, s, :, 3 * D:4 * D]).then_inc(e["keep"], 1)
            pairs(act, NG, group)
            f = acc[0:TN, :, :]
            if n == 0:
                act.wait_ge(e["finv"], 1)
                act.activation(f[:, :, 2 * D:3 * D], f[:, :, 0:D], ACT.Silu).then_inc(e["fina"], 1)
            if n != 1:
                act.wait_ge(e["finv"], 2)
                act.activation(f[:, :, D:2 * D], f[:, :, 0:D], ACT.Square).then_inc(e["fina"], 1)
                act.wait_ge(e["finv"], 3)
                act.activation(stat[0:TN, 2, :], stat[0:TN, 1, :], ACT.Sqrt, bias=eps_t[0:TN, :],
                               scale=1.0 / D).then_inc(e["fina"], 1)

        def epilogue_dve(dve, n, link):
            e, m = epis[n], passes[n]
            if n == 0:
                link(nc.vector.tensor_scalar(rcount[0:TN, :], acc[0:TN, :, K * D], 1.0, None, ALU.max))
                link(nc.vector.reciprocal(rcount[0:TN, :], rcount[0:TN, :]))
            for free in ("tr", "z", "keep"):
                dve.sem_inc(e[free], 2)

            def group(c, s, i):
                rc = rcount[0:TN, bass.ds(c * GT, GT)]
                dve.wait_ge(e["tr"], c + 1)
                if n == 0:
                    nc.vector.tensor_tensor(cat[0:TN, s, :, 0:K * D], acc[0:TN, bass.ds(c * GT, GT), 0:K * D],
                                            rc[:, :, None].broadcast_to([TN, GT, K * D]), ALU.mult).then_inc(e["catv"], 1)
                    dve.wait_ge(e["tr"], c + 3)
                    nc.vector.tensor_copy(catT[:, s, 1], ptr[s][1][:, 0:GT * TN].rearrange("p (t q) -> p t q", t=GT)).then_inc(e["evv"], 1)
                else:
                    nc.vector.tensor_tensor(cat[0:TN, s, :, D:2 * D], acc[0:TN, bass.ds(c * GT, GT), D:2 * D],
                                            rc[:, :, None].broadcast_to([TN, GT, D]), ALU.mult).then_inc(e["catv"], 1)
                dve.wait_ge(e["mm"], c + 1)
                slot = (0, 2 * D, D)[n]
                o = acc[0:TN, bass.ds(c * GT, GT), slot:slot + D]
                nc.vector.tensor_tensor(o, pout[s][0:TN, 0:GT * D].rearrange("p (t d) -> p t d", t=GT),
                                        bias_t[0:TN, n, None, :].broadcast_to([TN, GT, D]), ALU.add).then_inc(e["z"], 1)
            pairs(dve, NG, group)
            f = acc[0:TN, :, :]
            a, b, c = (f[:, :, j * D:(j + 1) * D] for j in range(3))
            dve.wait_ge(e["z"], NG + 2)
            if n == 1:
                nc.vector.tensor_scalar(c, c, 0.0, None, ALU.max).then_inc(e["fin"], 1)
                dve.wait_ge(e["fin"], 1)
                return
            if n == 0:
                dve.wait_ge(e["keep"], NG + 2)
                nc.vector.tensor_tensor(a, a, b, ALU.add).then_inc(e["finv"], 1)
                dve.wait_ge(e["fina"], 1)
                link(nc.vector.tensor_tensor(a, b, c, ALU.add))
            else:
                link(nc.vector.tensor_tensor(a, a, b, ALU.add))
                dve.sem_inc(e["finv"], 1)
            link(nc.vector.tensor_reduce(stat[0:TN, 0, :], a, AX_X, ALU.add))
            link(nc.vector.tensor_scalar(stat[0:TN, 0, :], stat[0:TN, 0, :], 1.0 / D, None, ALU.mult))
            nc.vector.tensor_tensor(a, a, stat[0:TN, 0, :, None].broadcast_to([TN, NT, D]), ALU.subtract).then_inc(e["finv"], 1)
            dve.wait_ge(e["fina"], 2 if n == 0 else 1)
            dve.wait_ge(e["finv"], 2)
            nc.vector.tensor_reduce(stat[0:TN, 1, :], b, AX_X, ALU.add).then_inc(e["finv"], 1)
            dve.wait_ge(e["fina"], 3 if n == 0 else 2)
            link(nc.vector.reciprocal(stat[0:TN, 3, :], stat[0:TN, 2, :]))
            nc.vector.tensor_tensor(a, a, stat[0:TN, 3, :, None].broadcast_to([TN, NT, D]), ALU.mult).then_inc(e["fin"], 1)


        @block.sync
        def _(sp):
            nat = lambda a: a.rearrange("(q e) -> q e", q=CH)
            sp.dma_start(dst_nat.bitcast(I32), nat(dst)).then_inc(s_load, 16)
            sp.dma_start(attr_nat.rearrange("p e a -> p (e a)"),
                         attr.rearrange("(q e) a -> q (e a)", q=CH)).then_inc(s_attr, 16)
            sp.dma_start(src_nat.bitcast(I32), nat(src)).then_inc(s_src, 16)
            for h in range(2):
                sp.dma_start(w0[h * D:(h + 1) * D, 0, :], g[:, h * D:(h + 1) * D]).then_inc(s_wt, 16)
            sp.dma_start(w0[0:D, 1, :], g[:, 2 * D:3 * D]).then_inc(s_wt, 16)
            sp.dma_start(w0[D:P, 1, :], root_w).then_inc(s_wt, 16)
            for t, a, b in ((w1, w_self1, w_neigh1), (w2, w_self2, w_neigh2)):
                sp.dma_start(t[0:D, :], a).then_inc(s_wt, 16)
                sp.dma_start(t[D:P, :], b).then_inc(s_wt, 16)
            xg = x.rearrange("(t p) d -> p t d", p=TN)
            e = epis[0]

            def load_x(c, s, i):
                sp.wait_ge(e["tr"], c + 1)
                sp.wait_ge(e["keep"], c + 1)
                sp.dma_start(cat[0:TN, s, :, 3 * D:4 * D],
                             xg[:, bass.ds(c * GT, GT), :]).then_inc(e[f"x{s}"], 16)
            pairs(sp, NG, load_x)
            sp.wait_ge(epis[0]["fin"], 1)
            sp.dma_start(table1.rearrange("(t p) d -> p t d", p=TN), acc[0:TN, :, 0:D]).then_inc(s_table, 16)
            sp.wait_ge(epis[1]["fin"], 1)
            sp.dma_start(table2.rearrange("(t p) d -> p t d", p=TN), acc[0:TN, :, 2 * D:3 * D]).then_inc(s_table, 16)
            sp.wait_ge(epis[2]["fin"], 1)
            sp.dma_start(out.rearrange("(t p) d -> p t d", p=TN), acc[0:TN, :, 0:D]).then_inc(s_out, 16)
            sp.wait_ge(s_out, 16)

        @block.gpsimd
        def _(pool):
            nc.gpsimd.iota(iota[:], pattern=[[1, P]], base=0, channel_multiplier=0,
                           allow_small_or_imprecise_dtypes=True).then_inc(s_const, 1)
            nc.gpsimd.iota(pidx[:], pattern=[[1, 1]], base=0, channel_multiplier=1,
                           allow_small_or_imprecise_dtypes=True).then_inc(s_const, 1)
            nc.gpsimd.iota(tile_base[:], pattern=[[TN, NT]], base=0, channel_multiplier=0,
                           allow_small_or_imprecise_dtypes=True).then_inc(s_const, 1)
            pool.wait_ge(s_const, 3)
            for n, m in enumerate(passes):
                if n:
                    pool.wait_ge(s_table, 16 * n)

                def gather(c, s, i):
                    pool.wait_ge(m["idx"], c + 1)
                    pool.sem_inc(s_tick, 1)
                    pool.wait_ge(m["gfree"], c + 1)
                    pool.sem_inc(s_tick, 1)
                    for b in range(BC):
                        pool.indirect_dma_start(
                            out=gath[:, s, b, :], out_offset=None, in_=tables[n],
                            in_offset=bass.IndirectOffsetOnAxis(ap=idx[:, s, b:b + 1], axis=0),
                        ).then_inc(m[f"gath{s}"], 16)
                pairs(pool, CH, gather)

        @block.scalar
        def _(act):
            act.dma_start(musig[:, 0, :], mu.rearrange("k a -> (k a)").partition_broadcast(P)).then_inc(s_pre, 16)
            act.dma_start(musig[:, 1, :], sigma.rearrange("k a -> (k a)").partition_broadcast(P)).then_inc(s_pre, 16)
            for j, b in enumerate((bias, b1, b2)):
                act.dma_start(bias_t[:, j, :], b.partition_broadcast(P)).then_inc(s_wt, 16)
            act.wait_ge(s_attr, 16)
            act.wait_ge(s_v, 1)
            for j in range(K * A):
                if j:
                    act.wait_ge(s_sq, 2 * j)
                act.activation(sq_nat, attr_nat[:, :, j % A], ACT.Square,
                               bias=consts[0:CH, 0, j:j + 1]).then_inc(s_sq, 1)
            act.wait_ge(s_sq, 2 * K * A)
            for k in range(K):
                act.activation(w_nat[:, k, :], w_nat[:, k, :], ACT.Exp).then_inc(s_nat[2 + k], 1)
            for n, (f, k, m) in enumerate(evs):
                if n % 2:
                    evacuate(act, n, f, k, m, s_eva)
            act.wait_ge(s_evv, (len(evs) + 1) // 2)
            act.wait_ge(s_eva, len(evs) // 2)
            for n, m in enumerate(passes):
                def copy_idx(c, s, i):
                    act.wait_ge(m["gfree"], c + 1)
                    act.copy(idx[:, s, :], src_col[:, bass.ds(c * BC, BC)]).then_inc(m["idx"], 1)
                pairs(act, CH, copy_idx)
                epilogue_act(act, n)

        @block.tensor
        def _(pe):
            pe.wait_ge(s_v, 4)
            for n, (f, k, m) in enumerate(evs):
                if k == 0:
                    pe.wait_ge(s_nat[f], 1)
                if n >= 4:
                    pe.wait_ge(s_eva if n % 2 else s_evv, (n - 4) // 2 + 1)
                for j in range(m):
                    t = pe.transpose(banks[n % 4][:, j * CH:(j + 1) * CH],
                                     nats[f][:, (k + j) * P:(k + j + 1) * P], ident[0:CH, 0:CH])
                t.then_inc(s_tr, 1)
            pe.wait_ge(s_wp, 1)
            for j, (c, r) in enumerate(((0, ident), (1, ident), (1, later))):
                t = pe.matmul(sums[0:1, j * P:j * P + CH], win[0:CH, c:c + 1], r[0:CH, 0:CH], start=True, stop=True)
            t.then_inc(s_wp, 1)
            pe.wait_ge(s_tab, 1)
            for n, m in enumerate(passes):
                width = AW if n == 0 else D

                def chunk(c, s, i):
                    many = pe.value_load(win_tab[0:1, 1, bass.ds(c, 1)], min_val=1, max_val=NT)
                    before = pe.value_load(win_tab[0:1, 2, bass.ds(c, 1)], min_val=0, max_val=NT * CH)
                    with pe.Fori(0, many, 1) as w:
                        k = before + w
                        if n:
                            pe.wait_ge(m[f"gath{s}"], 16 * BC * (i + 1))
                        pe.wait_ge(m["added"], k + 1)
                        for t in range(NS):
                            if n == 0:
                                pe.wait_ge(m["wg"], c * NS + t + 1)
                            pe.wait_ge(m["oh"], k * NS + t + 1)
                            for b in range(SB):
                                moving = wgath[:, t * SB + b, :] if n == 0 else gath[:, s, t * SB + b, :]
                                mm = pe.matmul(sums[0:TN, 0:width], onehot[:, t, b, 0:TN], moving,
                                               start=(t == 0 and b == 0), stop=(t == NS - 1 and b == SB - 1))
                            mm.then_inc(m["ohused"], 1)
                pairs(pe, CH, chunk)

                e = epis[n]
                pe.wait_ge(s_wt, 16 * 11)
                weights = [[w0[:, 0, :], w0[:, 1, :]], [w1[:]], [w2[:]]][n]

                def group(c, s, i):
                    if n:
                        pe.wait_ge(e["cata"], c + 1)
                    else:
                        pe.wait_ge(e[f"x{s}"], 16 * (i + 1))
                    pe.wait_ge(e["catv"], c + 1)
                    for h in range(len(weights)):
                        for t in range(GT):
                            mm = pe.transpose(ptr[s][h][:, t * TN:(t + 1) * TN],
                                              cat[0:TN, s, t, h * P:(h + 1) * P], ident[0:TN, 0:TN])
                    mm.then_inc(e["tr"], 1)
                    pe.wait_ge(e["eva"], c + 1)
                    if n == 0:
                        pe.wait_ge(e["evv"], c + 1)
                    pe.wait_ge(e["z"], c + 1)
                    for t in range(GT):
                        for h in range(len(weights)):
                            mm = pe.matmul(pout[s][0:TN, t * D:(t + 1) * D], catT[:, s, h, t, :], weights[h],
                                           start=(h == 0), stop=(h == len(weights) - 1))
                    mm.then_inc(e["mm"], 1)
                pairs(pe, NG, group)

        @block.vector
        def _(dve):
            chain = [0]

            def link(ins):
                chain[0] += 1
                ins.then_inc(s_v, 1)
                dve.wait_ge(s_v, chain[0])

            def bc(ap, dims):
                return ap.broadcast_to(dims)

            dve.wait_ge(s_pre, 32)
            link(nc.vector.tensor_scalar(consts[:, 0, :], musig[:, 0, :], -1.0, None, ALU.mult))
            link(nc.vector.tensor_tensor(consts[:, 1, :], musig[:, 1, :], musig[:, 1, :], ALU.mult))
            dve.wait_ge(s_const, 3)
            nc.vector.tensor_scalar(consts[:, 2, :], consts[:, 1, :], SIGMA_EPS, -2.0, ALU.add, ALU.mult)
            nc.vector.memset(eps_t[:], LN_EPS)
            link(nc.vector.tensor_scalar(ident[:], iota[:], pidx[:, 0:1], None, ALU.is_equal))
            nc.vector.reciprocal(consts[:, 3, :], consts[:, 2, :])
            link(nc.vector.tensor_scalar(later[:], iota[:], pidx[:, 0:1], None, ALU.is_gt))
            dve.wait_ge(s_load, 16)
            nc.vector.tensor_copy(dst_nat, dst_nat.bitcast(I32)).then_inc(s_nat[1], 1)
            dve.wait_ge(s_src, 16)
            nc.vector.tensor_copy(src_nat, src_nat.bitcast(I32)).then_inc(s_nat[0], 1)
            for j in range(K * A):
                k, a = divmod(j, A)
                dve.wait_ge(s_sq, 2 * j + 1)
                if a == 0:
                    nc.vector.tensor_scalar(w_nat[:, k, :], sq_nat, consts[0:CH, 3, j:j + 1], None,
                                            ALU.mult).then_inc(s_sq, 1)
                else:
                    nc.vector.scalar_tensor_tensor(w_nat[:, k, :], sq_nat, consts[0:CH, 3, j:j + 1],
                                                   w_nat[:, k, :], ALU.mult, ALU.add).then_inc(s_sq, 1)
            dve.wait_ge(s_nat[1], 1)
            nc.vector.tensor_reduce(span[0:CH, 0:1], dst_nat, AX_X, ALU.min)
            link(nc.vector.tensor_reduce(span[0:CH, 1:2], dst_nat, AX_X, ALU.max))
            link(nc.vector.tensor_scalar(sq_t[0:CH], span[0:CH], 1.0 / TN, None, ALU.mult))
            link(nc.vector.tensor_copy(spi[0:CH], sq_t[0:CH]))
            link(nc.vector.tensor_copy(sq_t[0:CH], spi[0:CH]))
            for _ in range(1):
                link(nc.vector.scalar_tensor_tensor(fix[0:CH], sq_t[0:CH], float(TN), span[0:CH], ALU.mult, ALU.is_gt))
                link(nc.vector.tensor_tensor(sq_t[0:CH], sq_t[0:CH], fix[0:CH], ALU.subtract))
                link(nc.vector.tensor_scalar(fix[0:CH], sq_t[0:CH], float(TN), float(TN), ALU.mult, ALU.add))
                link(nc.vector.tensor_tensor(fix[0:CH], fix[0:CH], span[0:CH], ALU.is_le))
                link(nc.vector.tensor_tensor(sq_t[0:CH], sq_t[0:CH], fix[0:CH], ALU.add))
            link(nc.vector.tensor_copy(win[0:CH, 0:1], sq_t[0:CH, 0:1]))
            link(nc.vector.tensor_tensor(win[0:CH, 1:2], sq_t[0:CH, 1:2], sq_t[0:CH, 0:1], ALU.subtract))
            nc.vector.tensor_scalar(win[0:CH, 1:2], win[0:CH, 1:2], 1.0, None, ALU.add).then_inc(s_wp, 1)
            for n, (f, k, m) in enumerate(evs):
                if n % 2 == 0:
                    evacuate(dve, n, f, k, m, s_evv)
            dve.wait_ge(s_wp, 2)
            nc.vector.tensor_copy(win_tab[0:1, :, 0:CH], sums[0:1, 0:3 * P].rearrange("o (j c) -> o j c", j=3)[:, :, 0:CH]).then_inc(s_tab, 1)
            dve.wait_ge(s_tab, 1)
            dve.wait_ge(s_evv, (len(evs) + 1) // 2)
            dve.wait_ge(s_eva, len(evs) // 2)

            for n, m in enumerate(passes):
                lo, width = (0, AW) if n == 0 else (D, D)
                if n == 0:
                    nc.vector.memset(wgath[:, :, K * D:AW], 1.0)
                for _ in range(2):
                    dve.sem_inc(m["gfree"], 1)
                nc.vector.memset(acc[0:TN, :, lo:lo + width], 0.0).then_inc(m["added"], 1)

                def chunk(c, s, i):
                    first = dve.value_load(win_tab[0:1, 0, bass.ds(c, 1)], min_val=0, max_val=NT - 1)
                    many = dve.value_load(win_tab[0:1, 1, bass.ds(c, 1)], min_val=1, max_val=NT)
                    before = dve.value_load(win_tab[0:1, 2, bass.ds(c, 1)], min_val=0, max_val=NT * CH)
                    if n == 0:
                        dve.wait_ge(m[f"gath{s}"], 16 * BC * (i + 1))
                        for t in range(NS):
                            sl = slice(t * SB, (t + 1) * SB)
                            w = w_col[:, :, bass.ds(c * BC + t * SB, SB)].rearrange("p k b -> p b k")
                            wg = nc.vector.tensor_tensor(
                                wgath[:, sl, 0:K * D].rearrange("p b (k d) -> p b k d", k=K),
                                gath[:, s, sl, :][:, :, None, :].broadcast_to([P, SB, K, D]),
                                w[:, :, :, None].broadcast_to([P, SB, K, D]), ALU.mult)
                            wg.then_inc(m["wg"], 1)
                        dve.wait_ge(m["wg"], NS * (c + 1))
                        dve.sem_inc(m["gfree"], 1)
                    with dve.Fori(0, many, 1) as w:
                        k = before + w
                        tile = nc.s_assert_within(first + w, 0, NT - 1,
                                                  skip_runtime_bounds_check_because="first + many <= NT")
                        nc.vector.tensor_scalar(local[:], dst_col[:, bass.ds(c * BC, BC)],
                                                tile_base[:, bass.ds(tile, 1)], None,
                                                ALU.subtract).then_inc(m["local"], 1)
                        dve.wait_ge(m["local"], k + 1)
                        for t in range(NS):
                            nc.vector.tensor_tensor(
                                onehot[:, t, :, 0:TN],
                                iota[:, None, 0:TN].broadcast_to([P, SB, TN]),
                                local[:, t * SB:(t + 1) * SB, None].broadcast_to([P, SB, TN]),
                                ALU.is_equal).then_inc(m["oh"], 1)
                        dve.wait_ge(m["ohused"], NS * (k + 1))
                        dve.wait_ge(m["added"], k + 1)
                        a = acc[0:TN, bass.ds(tile, 1), lo:lo + width].rearrange("p t d -> p (t d)")
                        nc.vector.tensor_tensor(a, sums[0:TN, 0:width], a, ALU.add).then_inc(m["added"], 1)
                    if n:
                        dve.wait_ge(m["added"], before + many + 1)
                        dve.sem_inc(m["gfree"], 1)
                pairs(dve, CH, chunk)
                total = dve.value_load(win_tab[0:1, 2, CH - 1:CH], min_val=0, max_val=NT * CH) + \
                    dve.value_load(win_tab[0:1, 1, CH - 1:CH], min_val=1, max_val=NT)
                dve.wait_ge(m["added"], total + 1)
                dve.sem_inc(m["done"], 1)
                epilogue_dve(dve, n, link)



_INS = ["x", "src", "dst", "edge_attr_3", "L0_gnn_g", "L0_gnn_mu", "L0_gnn_sigma", "L0_gnn_root_w", "L0_gnn_bias",
        "L1_gnn_W_self1", "L1_gnn_W_neigh1", "L1_gnn_b1", "L1_gnn_W_self2", "L1_gnn_W_neigh2", "L1_gnn_b2"]


def kernel(**inputs):
    import numpy as np
    import concourse.bacc as bacc
    from concourse.bass_utils import run_bass_kernel_spmd

    nc = bacc.Bacc("TRN2", target_bir_lowering=False, num_devices=1)
    arrays, args = {}, []
    for name in _INS:
        a = np.ascontiguousarray(inputs[name])
        arrays[f"in_{name}"] = a
        args.append(nc.dram_tensor(f"in_{name}", a.shape, mybir.dt.from_np(a.dtype), kind="ExternalInput").ap())
    shape = arrays["in_x"].shape
    args.append(nc.dram_tensor("out", shape, F32, kind="ExternalOutput").ap())
    gnn_kernel(nc, *args)
    r = run_bass_kernel_spmd(nc, [arrays], core_ids=[0])
    return r.results[0]["out"]
```
